# Optimizing a Trainium2 kernel written in Bass

```python
import numpy as np
import jax
import jax.numpy as jnp

def _softmax(x, axis=-1):
    return jax.nn.softmax(x, axis=axis)

def _gelu(x):
    return jax.nn.gelu(x, approximate=True)

def _silu(x):
    return jax.nn.silu(x)

def _sigmoid(x):
    return jax.nn.sigmoid(x)

def _layernorm(x, axis=-1, eps=1e-05):
    m = jnp.mean(x, axis=axis, keepdims=True)
    v = jnp.var(x, axis=axis, keepdims=True)
    return (x - m) / jnp.sqrt(v + eps)

def _scatter_add(tgt, idx, src, axis=0):
    return tgt.at[idx].add(src)

def _segment_sum(src, seg, n):
    return jax.ops.segment_sum(src, seg, n)
kernel_name = 'mk_adj_resnorm_d1_adj_r2_ec4b5b'

def setup_inputs(seed: int=0):
    np.random.seed(seed)
    _w = jnp.asarray

    def _rec_inputs():
        import jax
        import jax.numpy as jnp
        _gk = jax.random.key(seed)
        x = -0.0005207 + 1.001 * jax.random.normal(jax.random.fold_in(_gk, 1), (4096, 128), jnp.float32)
        _a = jax.random.bernoulli(jax.random.fold_in(_gk, 2), 0.00195312, (4096, 4096))
        _a = jnp.logical_or(_a, jnp.swapaxes(_a, -1, -2))
        _a = jnp.logical_or(_a, jnp.eye(4096, dtype=bool))
        _af = _a.astype(jnp.float32)
        _af = _af * jax.random.uniform(jax.random.fold_in(_gk, 3), (4096, 4096), jnp.float32, 0.05, 1)
        adj = _af
        return (x, adj)
    x, adj = _rec_inputs()

    def _L0_gnn_setup():
        import jax, jax.numpy as jnp
        import numpy as np
        N = 4096
        D = 128
        L = 3

        def _cxin_conv(x, a, eps, W, b):
            ax = a @ x
            h = ax + (1.0 + eps[0]) * ax
            for i in range(L):
                h = jax.nn.relu(h @ W[i].T + b[i])
            return h
        key = jax.random.key(seed)
        ks = jax.random.split(key, 8)
        s = 1.0 / np.sqrt(D)
        return {'x1': jax.random.normal(ks[0], (N, D), jnp.float32), 'x2': jax.random.normal(ks[1], (N, D), jnp.float32), 'G1': jax.random.uniform(ks[2], (N, N), jnp.float32), 'G2': jax.random.uniform(ks[3], (N, N), jnp.float32), 'eps1': jnp.zeros((1,), jnp.float32), 'eps2': jnp.zeros((1,), jnp.float32), 'W1': jax.random.normal(ks[4], (L, D, D), jnp.float32) * s, 'b1': jnp.zeros((L, D), jnp.float32), 'W2': jax.random.normal(ks[5], (L, D, D), jnp.float32) * s, 'b2': jnp.zeros((L, D), jnp.float32), 'Wm': jax.random.normal(ks[6], (D, 2 * D), jnp.float32) * (1.0 / np.sqrt(2 * D)), 'bm': jnp.zeros((D,), jnp.float32)}
    _L0_gnn_all = _L0_gnn_setup()
    _L0_gnn_in = {k: v for k, v in _L0_gnn_all.items() if k in ('x2', 'eps1', 'eps2', 'W1', 'b1', 'W2', 'b2', 'Wm', 'bm')}
    del _L0_gnn_all
    return {'x': x, 'adj': adj, 'L0_gnn_x2': _L0_gnn_in['x2'], 'L0_gnn_eps1': _L0_gnn_in['eps1'], 'L0_gnn_eps2': _L0_gnn_in['eps2'], 'L0_gnn_W1': _L0_gnn_in['W1'], 'L0_gnn_b1': _L0_gnn_in['b1'], 'L0_gnn_W2': _L0_gnn_in['W2'], 'L0_gnn_b2': _L0_gnn_in['b2'], 'L0_gnn_Wm': _L0_gnn_in['Wm'], 'L0_gnn_bm': _L0_gnn_in['bm']}

def reference(x, adj, L0_gnn_x2, L0_gnn_eps1, L0_gnn_eps2, L0_gnn_W1, L0_gnn_b1, L0_gnn_W2, L0_gnn_b2, L0_gnn_Wm, L0_gnn_bm):
    import jax
    import jax.numpy as jnp

    def _L0_gnn_ref(x1, x2, G1, G2, eps1, eps2, W1, b1, W2, b2, Wm, bm):
        import jax, jax.numpy as jnp
        import numpy as np
        N = 4096
        D = 128
        L = 3

        def _cxin_conv(x, a, eps, W, b):
            ax = a @ x
            h = ax + (1.0 + eps[0]) * ax
            for i in range(L):
                h = jax.nn.relu(h @ W[i].T + b[i])
            return h
        out1 = _cxin_conv(x1, G1, eps1, W1, b1)
        out2 = _cxin_conv(x2, G2, eps2, W2, b2)
        merged = jnp.concatenate((out1, out2), axis=1)
        return merged @ Wm.T + bm
    x = _layernorm(x + _L0_gnn_ref(x, L0_gnn_x2, adj, adj, L0_gnn_eps1, L0_gnn_eps2, L0_gnn_W1, L0_gnn_b1, L0_gnn_W2, L0_gnn_b2, L0_gnn_Wm, L0_gnn_bm), axis=-1)
    return x

_drawn_inputs = setup_inputs


def setup_inputs(seed=0):
    import zlib

    import numpy as np

    out = dict(_drawn_inputs(seed))
    spreads = {'L0_gnn_b1': (0.0, 0.1), 'L0_gnn_b2': (0.0, 0.1), 'L0_gnn_bm': (0.0, 0.1)}
    factors = {}
    for name, (base, spread) in spreads.items():
        noise = np.random.default_rng([zlib.crc32(name.encode()), seed]).standard_normal(out[name].shape)
        drawn = base * np.exp(spread * noise) if base else spread * noise
        out[name] = jnp.asarray(drawn.astype(out[name].dtype))
    for name, factor in factors.items():
        out[name] = (out[name] * factor).astype(out[name].dtype)
    return out
```

```python
import concourse.bass as bass
from concourse import mybir
from contextlib import ExitStack

P = 128


def graph_layer_kernel(nc, x1, adj, x2, eps1, eps2, w1, b1, w2, b2, wm, bm, out):
    F32, F32R = mybir.dt.float32, mybir.dt.float32r
    ALU, ACT = mybir.AluOpType, mybir.ActivationFunctionType

    CHUNKS, GROUPS, _, GK, CT, _ = adj.shape
    N, D = x1.shape
    TILES = N // P
    CW = CT * P
    LAYERS = w1.shape[1]
    RAW, SPLIT = 4, 8
    XT = 2 * GK
    PIECES = TILES // XT
    XRAW2 = 4
    EPS = 1e-5

    out_chunks = out.rearrange("(p c t) d -> c p t d", p=P, t=CT)
    x1_tiles = x1.rearrange("(p t) d -> p t d", p=P)
    x2_tiles = x2.rearrange("(p t) d -> p t d", p=P)

    ctx = ExitStack()
    with ctx:
        def sb(name, shape, dt=F32):
            return ctx.enter_context(nc.sbuf_tensor(name, shape, dt))

        def pb(name, shape):
            return ctx.enter_context(nc.psum_tensor(name, shape, F32))

        def sem(name):
            return ctx.enter_context(nc.semaphore(name))

        a_raw = sb("a_raw", [P, RAW, GK, CW])
        a_hi = sb("a_hi", [P, SPLIT, GK, CW], F32R)
        a_lo = sb("a_lo", [P, SPLIT, GK, CW], F32R)
        x_res = sb("x_res", [P, TILES, D])
        x2_raw = sb("x2_raw", [P, XRAW2, XT, D])
        x_hi = sb("x_hi", [P, 2, TILES, D], F32R)
        x_lo = sb("x_lo", [P, 2, TILES, D], F32R)
        w_raw = sb("w_raw", [P, 2 * LAYERS + 2, D])
        w_hi = sb("w_hi", [P, 2 * LAYERS + 2, D], F32R)
        w_lo = sb("w_lo", [P, 2 * LAYERS + 2, D], F32R)
        bias = sb("bias", [P, 2, LAYERS])
        eps_in = sb("eps_in", [P, 2])
        two_eps = sb("two_eps", [P, 2])
        bm_all = sb("bm_all", [P, D])
        var_eps = sb("var_eps", [P, 1])
        h = sb("h", [P, 2, CW])
        h_hi = sb("h_hi", [P, 2, CW], F32R)
        h_lo = sb("h_lo", [P, 2, CW], F32R)
        y = sb("y", [P, CT, D])
        y_out = sb("y_out", [P, CT, D])
        stats = sb("stats", [P, CT, 6])
        mean_var = sb("mean_var", [P, CT, 2])
        std = sb("std", [P, CT])
        rstd = sb("rstd", [P, CT])

        ps_ax = [pb(f"ps_ax{b}", [P, CW]) for b in range(2)]
        ps_z = [pb(f"ps_z{b}", [P, CW]) for b in range(2)]
        ps_m = pb("ps_m", [P, CW])

        raw_landed = [sem(f"raw_landed{s}") for s in range(RAW)]
        x_landed = [sem(f"x_landed{l}") for l in range(PIECES)]
        w_landed = sem("w_landed")
        small_landed = sem("small_landed")
        bm_landed = sem("bm_landed")
        stored = sem("stored")
        last_stored = sem("last_stored")
        x_hi_ready = sem("x_hi_ready")
        x_lo_ready = sem("x_lo_ready")
        x_res_ready = sem("x_res_ready")
        w_hi_ready = sem("w_hi_ready")
        w_lo_ready = sem("w_lo_ready")
        consts_ready = sem("consts_ready")
        hi_ready = sem("hi_ready")
        lo_ready = sem("lo_ready")
        group_used = sem("group_used")
        ax_done = sem("ax_done")
        z_done = sem("z_done")
        h_ready = sem("h_ready")
        h_hi_ready = sem("h_hi_ready")
        h_lo_ready = sem("h_lo_ready")
        m_done = sem("m_done")
        y_ready = sem("y_ready")
        stats_done = sem("stats_done")
        var_done = sem("var_done")
        std_done = sem("std_done")
        rstd_done = sem("rstd_done")
        y_out_ready = sem("y_out_ready")

        block = ctx.enter_context(nc.Block())

        @block.sync
        def _(sp):
            def load_chunk(c, first):
                for g in range(GROUPS):
                    if not (first and g < RAW):
                        sp.wait_ge(lo_ready, c * GROUPS + (g - RAW + 1))
                    src = adj[0, g] if first else adj[bass.ds(c, 1), g].rearrange("o p k t i -> p (o k t i)")
                    if first:
                        src = src.rearrange("p k t i -> p (k t i)")
                    sp.dma_start(a_raw[:, g % RAW].rearrange("p k j -> p (k j)"), src).then_inc(raw_landed[g % RAW], 16)

            load_chunk(0, True)
            with sp.Fori(1, CHUNKS) as c:
                load_chunk(c, False)

            sp.wait_ge(y_out_ready, CHUNKS)
            sp.dma_start(out_chunks[CHUNKS - 1], y_out[:]).then_inc(last_stored, 16)
            sp.wait_ge(stored, 16 * (CHUNKS - 1))
            sp.wait_ge(last_stored, 16)

        @block.gpsimd
        def _(pool):
            pool.dma_start(w_raw[:, 0:LAYERS], w1).then_inc(w_landed, 16)
            pool.dma_start(w_raw[:, LAYERS:2 * LAYERS], w2).then_inc(w_landed, 16)
            pool.dma_start(w_raw[:, 2 * LAYERS:], wm).then_inc(w_landed, 16)
            pool.dma_start(bias[:, 0], b1).then_inc(small_landed, 16)
            pool.dma_start(bias[:, 1], b2).then_inc(small_landed, 16)
            pool.dma_start(eps_in[:, 0:1], eps1[None, :].broadcast_to([P, 1])).then_inc(small_landed, 16)
            pool.dma_start(eps_in[:, 1:2], eps2[None, :].broadcast_to([P, 1])).then_inc(small_landed, 16)
            pool.dma_start(bm_all[:], bm[None, :].broadcast_to([P, D])).then_inc(bm_landed, 16)
            pool.wait_ge(bm_landed, 16)
            for l in range(PIECES):
                pool.wait_ge(x_lo_ready, l + 1)
                piece = x_res[:, l * XT:(l + 1) * XT, :]
                nc.gpsimd.tensor_tensor(piece, piece, bm_all[:, None, :].broadcast_to([P, XT, D]),
                                        ALU.add).then_inc(x_res_ready, 1)

            with pool.Fori(0, CHUNKS - 1) as c:
                pool.wait_ge(y_out_ready, c + 1)
                pool.dma_start(out_chunks[bass.ds(c, 1)].rearrange("o p t d -> p (o t d)"),
                               y_out[:].rearrange("p t d -> p (t d)")).then_inc(stored, 16)

        @block.scalar
        def _(act):
            def split_hi(c, g, first):
                act.wait_ge(raw_landed[g % RAW], (c * (GROUPS // RAW) + (g // RAW + 1)) * 16)
                if not (first and g < SPLIT):
                    act.wait_ge(group_used, c * GROUPS + (g - SPLIT + 1))
                nc.scalar.activation(a_hi[:, g % SPLIT], a_raw[:, g % RAW], ACT.Copy).then_inc(hi_ready, 1)

            def ax_hi(c):
                for b in range(2):
                    if b == 0:
                        act.wait_ge(ax_done, c + 1)
                    else:
                        act.wait_ge(group_used, c * GROUPS + GROUPS)
                    nc.scalar.activation(h_hi[:, b], ps_ax[b][:], ACT.Copy,
                                         scale=two_eps[:, b:b + 1]).then_inc(h_hi_ready, 1)

            def relu(c, l):
                for b in range(2):
                    act.wait_ge(z_done, c * (2 * LAYERS) + (2 * l + b + 1))
                    nc.scalar.activation(h[:, b], ps_z[b][:], ACT.Relu,
                                         bias=bias[:, b, l:l + 1]).then_inc(h_ready, 1)

            def std_dev(c):
                act.wait_ge(var_done, c + 1)
                nc.scalar.activation(std[:], mean_var[:, :, 1], ACT.Sqrt, bias=var_eps[:]).then_inc(std_done, 1)

            def load_x(l):
                act.dma_start(x_res[:, l * XT:(l + 1) * XT, :], x1_tiles[:, l * XT:(l + 1) * XT, :]).then_inc(x_landed[l], 16)
                act.dma_start(x2_raw[:, l % XRAW2], x2_tiles[:, l * XT:(l + 1) * XT, :]).then_inc(x_landed[l], 16)

            for l in range(XRAW2):
                load_x(l)
            for l in range(PIECES):
                act.wait_ge(x_landed[l], 32)
                nc.scalar.activation(x_hi[:, 0, l * XT:(l + 1) * XT, :], x_res[:, l * XT:(l + 1) * XT, :], ACT.Copy)
                nc.scalar.activation(x_hi[:, 1, l * XT:(l + 1) * XT, :], x2_raw[:, l % XRAW2], ACT.Copy).then_inc(x_hi_ready, 1)
                split_hi(0, 2 * l, True)
                split_hi(0, 2 * l + 1, True)
                if l == 0:
                    act.wait_ge(w_landed, 48)
                    nc.scalar.activation(w_hi[:], w_raw[:], ACT.Copy).then_inc(w_hi_ready, 1)
                    act.wait_ge(consts_ready, 2)
                    act.wait_ge(small_landed, 64)
                if 1 <= l <= PIECES - XRAW2:
                    act.wait_ge(x_lo_ready, l)
                    load_x(l - 1 + XRAW2)

            with act.Fori(1, CHUNKS) as c:
                split_hi(c, 0, False)
                split_hi(c, 1, False)
                ax_hi(c - 1)
                for l in range(LAYERS):
                    split_hi(c, 2 * l + 2, False)
                    split_hi(c, 2 * l + 3, False)
                    relu(c - 1, l)
                split_hi(c, 2 * LAYERS + 2, False)
                split_hi(c, 2 * LAYERS + 3, False)
                split_hi(c, 2 * LAYERS + 4, False)
                std_dev(c - 1)
                for g in range(2 * LAYERS + 5, GROUPS):
                    split_hi(c, g, False)
            ax_hi(CHUNKS - 1)
            for l in range(LAYERS):
                relu(CHUNKS - 1, l)
            std_dev(CHUNKS - 1)

        @block.vector
        def _(dve):
            def split_lo(c, g):
                dve.wait_ge(hi_ready, c * GROUPS + (g + 1))
                nc.vector.tensor_tensor(a_lo[:, g % SPLIT], a_raw[:, g % RAW], a_hi[:, g % SPLIT].bitcast(F32),
                                        ALU.subtract).then_inc(lo_ready, 1)

            def ax_lo(c):
                for b in range(2):
                    dve.wait_ge(h_hi_ready, c * (2 * LAYERS + 2) + (b + 1))
                    nc.vector.scalar_tensor_tensor(out=h_lo[:, b], in0=ps_ax[b][:], scalar=two_eps[:, b:b + 1],
                                                   in1=h_hi[:, b].bitcast(F32), op0=ALU.mult,
                                                   op1=ALU.subtract).then_inc(h_lo_ready, 1)

            def split_h(c, l):
                for b in range(2):
                    n = 2 * l + b + 1
                    dve.wait_ge(h_ready, c * (2 * LAYERS) + n)
                    nc.vector.tensor_copy(h_hi[:, b], h[:, b]).then_inc(h_hi_ready, 1)
                    dve.wait_ge(h_hi_ready, c * (2 * LAYERS + 2) + (2 + n))
                    nc.vector.tensor_tensor(h_lo[:, b], h[:, b], h_hi[:, b].bitcast(F32),
                                            ALU.subtract).then_inc(h_lo_ready, 1)

            def norm_stats(c, rows):
                dve.wait_ge(m_done, c + 1)
                nc.vector.tensor_tensor(y[:].rearrange("p t d -> p (t d)"), ps_m[:], rows, ALU.add).then_inc(y_ready, 1)
                dve.wait_ge(y_ready, c + 1)
                for t in range(CT):
                    last = nc.vector.bn_stats(stats[:, t, :], y[:, t, :])
                last.then_inc(stats_done, 1)

            def norm_var():
                for t in range(CT):
                    last = nc.vector.bn_aggr(mean_var[:, t, :], stats[:, t, :])
                last.then_inc(var_done, 1)

            def norm_apply(c, wait_store):
                dve.wait_ge(std_done, c + 1)
                nc.vector.reciprocal(rstd[:], std[:]).then_inc(rstd_done, 1)
                dve.wait_ge(rstd_done, c + 1)
                if wait_store:
                    dve.wait_ge(stored, c * 16)
                for t in range(CT):
                    last = nc.vector.tensor_scalar(y_out[:, t, :], y[:, t, :], mean_var[:, t, 0:1], rstd[:, t:t + 1],
                                                   ALU.subtract, ALU.mult)
                last.then_inc(y_out_ready, 1)

            def chunk_beside(c, wait_store):
                split_lo(c, 0)
                split_lo(c, 1)
                ax_lo(c - 1)
                for l in range(LAYERS):
                    split_lo(c, 2 * l + 2)
                    split_lo(c, 2 * l + 3)
                    split_h(c - 1, l)
                split_lo(c, 2 * LAYERS + 2)
                split_lo(c, 2 * LAYERS + 3)
                rows = x_res[:, bass.ds((c - 1) * CT, CT), :] if not isinstance(c, int) else x_res[:, (c - 1) * CT:c * CT, :]
                norm_stats(c - 1, rows.rearrange("p t d -> p (t d)"))
                dve.wait_ge(stats_done, c)
                split_lo(c, 2 * LAYERS + 4)
                norm_var()
                split_lo(c, 2 * LAYERS + 5)
                norm_apply(c - 1, wait_store)
                for g in range(2 * LAYERS + 6, GROUPS):
                    split_lo(c, g)

            nc.vector.memset(var_eps[:], EPS).then_inc(consts_ready, 1)
            for l in range(PIECES):
                dve.wait_ge(x_hi_ready, l + 1)
                piece = slice(l * XT, (l + 1) * XT)
                nc.vector.tensor_tensor(x_lo[:, 0, piece, :], x_res[:, piece, :], x_hi[:, 0, piece, :].bitcast(F32),
                                        ALU.subtract)
                nc.vector.tensor_tensor(x_lo[:, 1, piece, :], x2_raw[:, l % XRAW2], x_hi[:, 1, piece, :].bitcast(F32),
                                        ALU.subtract).then_inc(x_lo_ready, 1)
                split_lo(0, 2 * l)
                split_lo(0, 2 * l + 1)
                if l == 0:
                    dve.wait_ge(small_landed, 64)
                    nc.vector.tensor_scalar(two_eps[:], eps_in[:], 1.0, 1.0, ALU.add, ALU.add).then_inc(consts_ready, 1)
                    dve.wait_ge(consts_ready, 2)
                    dve.wait_ge(w_hi_ready, 1)
                    nc.vector.tensor_tensor(w_lo[:], w_raw[:], w_hi[:].bitcast(F32), ALU.subtract).then_inc(w_lo_ready, 1)
            dve.wait_ge(x_res_ready, PIECES)
            chunk_beside(1, False)
            with dve.Fori(2, CHUNKS) as c:
                chunk_beside(c, True)
            ax_lo(CHUNKS - 1)
            for l in range(LAYERS):
                split_h(CHUNKS - 1, l)
            norm_stats(CHUNKS - 1, x_res[:, (CHUNKS - 1) * CT:, :].rearrange("p t d -> p (t d)"))
            dve.wait_ge(stats_done, CHUNKS)
            norm_var()
            norm_apply(CHUNKS - 1, True)

        @block.tensor
        def _(pe):
            def matmul3(dst, w_parts, m_parts, start, stop):
                (wh, wl), (mh, ml) = w_parts, m_parts
                nc.tensor.matmul(dst, wh, mh, start=start, stop=False)
                nc.tensor.matmul(dst, wl, mh, start=False, stop=False)
                return nc.tensor.matmul(dst, wh, ml, start=False, stop=stop)

            def adj_pair(c, l, first):
                if first:
                    pe.wait_ge(x_lo_ready, l + 1)
                for b in range(2):
                    if l == 0 and not first:
                        pe.wait_ge(h_lo_ready, (c - 1) * (2 * LAYERS + 2) + (b + 1))
                    for g in (2 * l, 2 * l + 1):
                        if b == 0:
                            pe.wait_ge(lo_ready, c * GROUPS + (g + 1))
                        for k in range(GK):
                            t = g * GK + k
                            last = matmul3(ps_ax[b][:], (x_hi[:, b, t, :], x_lo[:, b, t, :]),
                                           (a_hi[:, g % SPLIT, k], a_lo[:, g % SPLIT, k]),
                                           t == 0, t == TILES - 1)
                        if b == 1:
                            last.then_inc(group_used, 1)
                        elif g == GROUPS - 1:
                            last.then_inc(ax_done, 1)

            def layer(c, l):
                for b in range(2):
                    pe.wait_ge(h_lo_ready, c * (2 * LAYERS + 2) + (2 * l + b + 1))
                    w = b * LAYERS + l
                    matmul3(ps_z[b][:], (w_hi[:, w, :], w_lo[:, w, :]), (h_hi[:, b], h_lo[:, b]),
                            True, True).then_inc(z_done, 1)

            def merge(c, first):
                pe.wait_ge(h_lo_ready, c * (2 * LAYERS + 2) + (2 * LAYERS + 2))
                if not first:
                    pe.wait_ge(y_ready, c)
                for t in range(CT):
                    cols = slice(t * P, (t + 1) * P)
                    for b in range(2):
                        w = 2 * LAYERS + b
                        last = matmul3(ps_m[:, cols], (h_hi[:, b, cols], h_lo[:, b, cols]),
                                       (w_hi[:, w, :], w_lo[:, w, :]), b == 0, b == 1)
                last.then_inc(m_done, 1)

            PAIRS = GROUPS // 2

            def chunk_beside(c, first_merge):
                adj_pair(c, 0, False)
                for l in range(LAYERS):
                    layer(c - 1, l)
                    adj_pair(c, l + 1, False)
                merge(c - 1, first_merge)
                for l in range(LAYERS + 1, PAIRS):
                    adj_pair(c, l, False)

            for l in range(PAIRS):
                adj_pair(0, l, True)
            pe.wait_ge(w_lo_ready, 1)
            chunk_beside(1, True)
            with pe.Fori(2, CHUNKS) as c:
                chunk_beside(c, False)
            for l in range(LAYERS):
                layer(CHUNKS - 1, l)
            merge(CHUNKS - 1, False)


def kernel(x, adj, L0_gnn_x2, L0_gnn_eps1, L0_gnn_eps2, L0_gnn_W1, L0_gnn_b1, L0_gnn_W2, L0_gnn_b2, L0_gnn_Wm,
           L0_gnn_bm):
    import numpy as np
    import concourse.bacc as bacc
    from concourse.bass_utils import run_bass_kernel_spmd

    n, d = x.shape
    tiles, chunk_tiles, group_tiles = n // P, 4, 2
    adj_blocks = np.asarray(adj).reshape(P, tiles // chunk_tiles, chunk_tiles, P, tiles // group_tiles, group_tiles)
    layers = lambda w: np.asarray(w).transpose(2, 0, 1)
    arrays = {
        "x": np.asarray(x),
        "adj": adj_blocks.transpose(1, 4, 3, 5, 2, 0),
        "x2": np.asarray(L0_gnn_x2),
        "eps1": np.asarray(L0_gnn_eps1),
        "eps2": np.asarray(L0_gnn_eps2),
        "w1": layers(L0_gnn_W1),
        "b1": np.asarray(L0_gnn_b1).T,
        "w2": layers(L0_gnn_W2),
        "b2": np.asarray(L0_gnn_b2).T,
        "wm": np.asarray(L0_gnn_Wm).reshape(d, 2, d).transpose(2, 1, 0),
        "bm": np.asarray(L0_gnn_bm),
    }
    arrays = {f"in_{k}": np.ascontiguousarray(v) for k, v in arrays.items()}
    nc = bacc.Bacc("TRN2", target_bir_lowering=False, num_devices=1)
    args = [nc.dram_tensor(k, v.shape, mybir.dt.from_np(v.dtype), kind="ExternalInput").ap() for k, v in arrays.items()]
    out = nc.dram_tensor("out", (n, d), mybir.dt.float32, kind="ExternalOutput").ap()
    graph_layer_kernel(nc, *args, out)
    r = run_bass_kernel_spmd(nc, [arrays], core_ids=[0])
    return r.results[0]["out"]
```

```python
import concourse.bass as bass
from concourse import mybir
from contextlib import ExitStack

P = 128


def graph_layer_kernel(nc, xs, adj, eps, w1, b1, w2, b2, wm, bm, out):
    F32, F32R, BF16 = mybir.dt.float32, mybir.dt.float32r, mybir.dt.bfloat16
    ALU, ACT = mybir.AluOpType, mybir.ActivationFunctionType

    CHUNKS, GROUPS, _, _ = adj.shape
    _, N, D = xs.shape
    TILES = N // P
    GK = TILES // GROUPS
    CT = TILES // CHUNKS
    CW = CT * P
    HT = CT // 2
    HW = HT * P
    LAYERS = w1.shape[1]
    RAW, SPLIT = 4, 8
    LAST = CHUNKS - 1
    EPS = 1e-5
    WARM = 10

    out_tiles = out.rearrange("(p t) d -> p t d", p=P)
    out_chunks = out.rearrange("(p c t) d -> c p t d", p=P, t=CT)
    x_tiles = xs.rearrange("b (p t) d -> p b t d", p=P)

    ctx = ExitStack()
    with ctx:
        def sb(name, shape, dt=F32):
            return ctx.enter_context(nc.sbuf_tensor(name, shape, dt))

        def pb(name, shape):
            return ctx.enter_context(nc.psum_tensor(name, shape, F32))

        def sem(name):
            return ctx.enter_context(nc.semaphore(name))

        a_raw = sb("a_raw", [P, RAW, GK * CW])
        a_hi = sb("a_hi", [P, SPLIT, GK * CW], F32R)
        a_lo = sb("a_lo", [P, SPLIT, GK * CW], F32R)
        x_raw = sb("x_raw", [P, 2, TILES, D])
        x_hi = sb("x_hi", [P, 2, TILES, D], F32R)
        x_lo = sb("x_lo", [P, 2, TILES, D], F32R)
        w_raw = sb("w_raw", [P, 2 * LAYERS + 2, D])
        w_hi = sb("w_hi", [P, 2 * LAYERS, D], F32R)
        w_lo = sb("w_lo", [P, 2 * LAYERS, D], F32R)
        wm_parts = sb("wm_parts", [P, 2, 2, D], F32R)
        bias = sb("bias", [P, 2, LAYERS])
        eps_in = sb("eps_in", [P, 2])
        two_eps = sb("two_eps", [P, 2])
        bm_all = sb("bm_all", [P, D])
        var_eps = sb("var_eps", [P, 1])
        table_warm = sb("table_warm", [P, 1])
        pe_warm = sb("pe_warm", [P, P], BF16)
        h = sb("h", [P, 2, CW])
        h_hi = sb("h_hi", [P, 2, CW], F32R)
        h_lo = sb("h_lo", [P, 2, CW], F32R)
        y = sb("y", [P, CT, D])
        y_out = sb("y_out", [P, CT, D])
        stats = sb("stats", [P, CT, 6])
        mean_var = sb("mean_var", [P, CT, 2])
        std = sb("std", [P, CT])
        rstd = sb("rstd", [P, CT])

        ps_ax = [pb(f"ps_ax{b}", [P, CW]) for b in range(2)]
        ps_z = [pb(f"ps_z{b}", [P, CW]) for b in range(2)]
        ps_m = pb("ps_m", [P, CT, 2, D])
        ps_ax_end = [pb(f"ps_ax_end{b}", [P, CW]) for b in range(2)]
        ps_m_end = ps_ax[0]

        x_landed = [sem(f"x_landed{g}") for g in range(GROUPS)]
        tile_landed = [sem(f"tile_landed{s}") for s in range(RAW * GK)]
        raw_landed = [sem(f"raw_landed{s}") for s in range(RAW)]
        w_landed = sem("w_landed")
        small_landed = sem("small_landed")
        bm_landed = sem("bm_landed")
        stored = sem("stored")
        last_stored = sem("last_stored")
        x_hi_ready = sem("x_hi_ready")
        x_lo_ready = sem("x_lo_ready")
        x_res_ready = sem("x_res_ready")
        w_hi_ready = sem("w_hi_ready")
        w_lo_ready = sem("w_lo_ready")
        const_ready = sem("const_ready")
        two_eps_ready = sem("two_eps_ready")
        pe_warm_ready = sem("pe_warm_ready")
        hi_ready = sem("hi_ready")
        lo_ready = sem("lo_ready")
        group_used = sem("group_used")
        ax_done = sem("ax_done")
        z_done = sem("z_done")
        h_ready = sem("h_ready")
        h_hi_ready = sem("h_hi_ready")
        h_lo_ready = sem("h_lo_ready")
        m_done = sem("m_done")
        y_hi_done = sem("y_hi_done")
        y_ready = sem("y_ready")
        stats_done = sem("stats_done")
        var_done = sem("var_done")
        std_done = sem("std_done")
        rstd_done = sem("rstd_done")
        y_out_ready = sem("y_out_ready")
        end_h_ready = [sem(f"end_h_ready{b}") for b in range(2)]
        end_z_done = [sem(f"end_z_done{b}") for b in range(2)]

        def split_count(c, g):
            return c * GROUPS + (TILES - GROUPS + g + 1)

        block = ctx.enter_context(nc.Block())

        @block.sync
        def _(sp):
            for g in range(GROUPS):
                tiles = slice(g * GK, (g + 1) * GK)
                sp.dma_start(x_raw[:, :, tiles, :], x_tiles[:, :, tiles, :]).then_inc(x_landed[g], 16)
                if g >= RAW:
                    sp.wait_ge(lo_ready, (g - RAW + 1) * GK)
                for k in range(GK):
                    sp.dma_start(a_raw[:, g % RAW, k * CW:(k + 1) * CW],
                                 adj[0, g, :, k * CW:(k + 1) * CW]).then_inc(tile_landed[g % RAW * GK + k], 16)

            with sp.Fori(1, LAST) as c:
                for g in range(GROUPS):
                    sp.wait_ge(lo_ready, split_count(c, g - RAW))
                    sp.dma_start(a_raw[:, g % RAW], adj[bass.ds(c, 1), g].rearrange("o p n -> p (o n)")).then_inc(raw_landed[g % RAW], 16)

            for g in range(GROUPS):
                sp.wait_ge(lo_ready, split_count(LAST, g - RAW))
                sp.dma_start(a_raw[:, g % RAW], adj[LAST, g]).then_inc(raw_landed[g % RAW], 16)

            for half in range(2):
                sp.wait_ge(y_out_ready, LAST + half + 1)
                tiles = slice(half * HT, (half + 1) * HT)
                sp.dma_start(out_chunks[LAST, :, tiles, :], y_out[:, tiles, :]).then_inc(last_stored, 16)
            sp.wait_ge(stored, 16 * LAST)
            sp.wait_ge(last_stored, 32)

        @block.gpsimd
        def _(pool):
            pool.wait_ge(x_hi_ready, 2)
            pool.dma_start(w_raw[:, 0:LAYERS], w1).then_inc(w_landed, 16)
            pool.dma_start(w_raw[:, LAYERS:2 * LAYERS], w2).then_inc(w_landed, 16)
            pool.dma_start(w_raw[:, 2 * LAYERS:], wm).then_inc(w_landed, 16)
            pool.dma_start(bias[:, 0], b1).then_inc(small_landed, 16)
            pool.dma_start(bias[:, 1], b2).then_inc(small_landed, 16)
            pool.dma_start(eps_in[:], eps[None, :].broadcast_to([P, 2])).then_inc(small_landed, 16)
            pool.dma_start(bm_all[:], bm[None, :].broadcast_to([P, D])).then_inc(bm_landed, 16)
            pool.wait_ge(bm_landed, 16)
            for c in range(CHUNKS):
                pool.wait_ge(x_lo_ready, (c + 1) * CT // GK)
                rows = x_raw[:, 0, c * CT:(c + 1) * CT, :]
                nc.gpsimd.tensor_tensor(rows, rows, bm_all[:, None, :].broadcast_to([P, CT, D]),
                                        ALU.add).then_inc(x_res_ready, 1)

            with pool.Fori(0, LAST) as c:
                pool.wait_ge(y_out_ready, c + 1)
                pool.dma_start(out_chunks[bass.ds(c, 1)].rearrange("o p t d -> p (o t d)"),
                               y_out[:].rearrange("p t d -> p (t d)")).then_inc(stored, 16)

        @block.scalar
        def _(act):
            def split_hi(c, g):
                act.wait_ge(raw_landed[g % RAW], (c * (GROUPS // RAW) + (g // RAW + 1 - GROUPS // RAW)) * 16)
                act.wait_ge(group_used, c * GROUPS + (g - SPLIT + 1))
                nc.scalar.activation(a_hi[:, g % SPLIT], a_raw[:, g % RAW], ACT.Copy).then_inc(hi_ready, 1)

            def ax_hi(s, last_group, w):
                for b in range(2):
                    if b == 0:
                        act.wait_ge(ax_done, s + 1)
                    else:
                        act.wait_ge(group_used, last_group)
                    nc.scalar.activation(h_hi[:, b, 0:w], ps_ax[b][:, 0:w], ACT.Copy,
                                         scale=two_eps[:, b:b + 1]).then_inc(h_hi_ready, 1)

            def relu(s, l, w):
                for b in range(2):
                    act.wait_ge(z_done, s * (2 * LAYERS) + (2 * l + b + 1))
                    nc.scalar.activation(h[:, b, 0:w], ps_z[b][:, 0:w], ACT.Relu,
                                         bias=bias[:, b, l:l + 1]).then_inc(h_ready, 1)

            def std_dev(s, tiles):
                act.wait_ge(var_done, s + 1)
                nc.scalar.activation(std[:, tiles], mean_var[:, tiles, 1], ACT.Sqrt,
                                     bias=var_eps[:]).then_inc(std_done, 1)

            act.wait_ge(const_ready, 1)
            nc.scalar.activation(table_warm[:], var_eps[:], ACT.Sqrt)

            for g in range(GROUPS):
                tiles = slice(g * GK, (g + 1) * GK)
                act.wait_ge(x_landed[g], 16)
                nc.scalar.activation(x_hi[:, :, tiles, :], x_raw[:, :, tiles, :], ACT.Copy).then_inc(x_hi_ready, 1)
                for k in range(GK):
                    act.wait_ge(tile_landed[g % RAW * GK + k], (g // RAW + 1) * 16)
                    if g >= SPLIT and k == 0:
                        act.wait_ge(group_used, g - SPLIT + 1)
                    cols = slice(k * CW, (k + 1) * CW)
                    nc.scalar.activation(a_hi[:, g % SPLIT, cols], a_raw[:, g % RAW, cols],
                                         ACT.Copy).then_inc(hi_ready, 1)
                if g == GROUPS - 2:
                    act.wait_ge(w_landed, 48)
                    nc.scalar.activation(w_hi[:], w_raw[:, 0:2 * LAYERS], ACT.Copy)
                    nc.scalar.activation(wm_parts[:, :, 0, :], w_raw[:, 2 * LAYERS:], ACT.Copy).then_inc(w_hi_ready, 1)
                    act.wait_ge(small_landed, 48)
                    act.wait_ge(two_eps_ready, 1)

            with act.Fori(1, LAST) as c:
                split_hi(c, 0)
                split_hi(c, 1)
                ax_hi(c - 1, c * GROUPS, CW)
                for l in range(LAYERS):
                    split_hi(c, 2 * l + 2)
                    split_hi(c, 2 * l + 3)
                    relu(c - 1, l, CW)
                for g in range(2 * LAYERS + 2, 2 * LAYERS + 7):
                    split_hi(c, g)
                std_dev(c - 1, slice(0, CT))
                for g in range(2 * LAYERS + 7, GROUPS):
                    split_hi(c, g)

            for half, (s, w) in enumerate(((LAST - 1, CW), (LAST, HW))):
                g = half * (GROUPS // 2)
                split_hi(LAST, g)
                split_hi(LAST, g + 1)
                if half == 1:
                    act.wait_ge(m_done, LAST)
                ax_hi(s, LAST * GROUPS + g, w)
                for l in range(LAYERS):
                    split_hi(LAST, g + 2 * l + 2)
                    split_hi(LAST, g + 2 * l + 3)
                    if half == 1 and l == 0:
                        std_dev(LAST - 1, slice(0, CT))
                    relu(s, l, w)

            act.wait_ge(ax_done, LAST + 2)
            nc.scalar.activation(h[:, 0, HW:], ps_ax_end[0][:, 0:HW], ACT.Copy,
                                 scale=two_eps[:, 0:1]).then_inc(end_h_ready[0], 1)
            std_dev(LAST, slice(0, HT))
            for l in range(LAYERS):
                act.wait_ge(end_z_done[0], l + 1)
                nc.scalar.activation(h[:, 0, HW:], ps_z[0][:, HW:], ACT.Relu,
                                     bias=bias[:, 0, l:l + 1]).then_inc(end_h_ready[0], 1)
            std_dev(LAST + 1, slice(HT, CT))

        @block.vector
        def _(dve):
            def split_lo(c, g):
                dve.wait_ge(hi_ready, split_count(c, g))
                nc.vector.tensor_tensor(a_lo[:, g % SPLIT], a_raw[:, g % RAW], a_hi[:, g % SPLIT].bitcast(F32),
                                        ALU.subtract).then_inc(lo_ready, 1)

            def ax_lo(s, w):
                for b in range(2):
                    dve.wait_ge(h_hi_ready, s * (2 * LAYERS + 2) + (b + 1))
                    nc.vector.scalar_tensor_tensor(out=h_lo[:, b, 0:w], in0=ps_ax[b][:, 0:w],
                                                   scalar=two_eps[:, b:b + 1], in1=h_hi[:, b, 0:w].bitcast(F32),
                                                   op0=ALU.mult, op1=ALU.subtract).then_inc(h_lo_ready, 1)

            def split_h(s, l, w):
                for b in range(2):
                    n = 2 * l + b + 1
                    dve.wait_ge(h_ready, s * (2 * LAYERS) + n)
                    nc.vector.tensor_copy(h_hi[:, b, 0:w], h[:, b, 0:w]).then_inc(h_hi_ready, 1)
                    dve.wait_ge(h_hi_ready, s * (2 * LAYERS + 2) + (2 + n))
                    nc.vector.tensor_tensor(h_lo[:, b, 0:w], h[:, b, 0:w], h_hi[:, b, 0:w].bitcast(F32),
                                            ALU.subtract).then_inc(h_lo_ready, 1)

            def norm_sum(s, rows, tiles):
                dve.wait_ge(m_done, s + 1)
                nc.vector.tensor_tensor(y[:, tiles, :], ps_m[:, tiles, 0, :], rows, ALU.add).then_inc(y_hi_done, 1)
                dve.wait_ge(y_hi_done, s + 1)
                nc.vector.tensor_tensor(y[:, tiles, :], ps_m[:, tiles, 1, :], y[:, tiles, :], ALU.add).then_inc(y_ready, 1)

            def norm_stats(s, tiles):
                dve.wait_ge(y_ready, s + 1)
                for t in range(tiles.start, tiles.stop):
                    last = nc.vector.bn_stats(stats[:, t, :], y[:, t, :])
                last.then_inc(stats_done, 1)

            def norm_var(tiles):
                for t in range(tiles.start, tiles.stop):
                    last = nc.vector.bn_aggr(mean_var[:, t, :], stats[:, t, :])
                last.then_inc(var_done, 1)

            def norm_apply(s, tiles):
                dve.wait_ge(std_done, s + 1)
                nc.vector.reciprocal(rstd[:, tiles], std[:, tiles]).then_inc(rstd_done, 1)
                dve.wait_ge(rstd_done, s + 1)
                for t in range(tiles.start, tiles.stop):
                    last = nc.vector.tensor_scalar(y_out[:, t, :], y[:, t, :], mean_var[:, t, 0:1], rstd[:, t:t + 1],
                                                   ALU.subtract, ALU.mult)
                last.then_inc(y_out_ready, 1)

            ALL, HALF, OTHER_HALF = slice(0, CT), slice(0, HT), slice(HT, CT)

            nc.vector.memset(pe_warm[:], 0.0).then_inc(pe_warm_ready, 1)
            nc.vector.memset(var_eps[:], EPS).then_inc(const_ready, 1)
            for g in range(GROUPS):
                tiles = slice(g * GK, (g + 1) * GK)
                dve.wait_ge(x_hi_ready, g + 1)
                nc.vector.tensor_tensor(x_lo[:, :, tiles, :], x_raw[:, :, tiles, :], x_hi[:, :, tiles, :].bitcast(F32),
                                        ALU.subtract).then_inc(x_lo_ready, 1)
                for k in range(GK):
                    dve.wait_ge(hi_ready, g * GK + k + 1)
                    cols = slice(k * CW, (k + 1) * CW)
                    nc.vector.tensor_tensor(a_lo[:, g % SPLIT, cols], a_raw[:, g % RAW, cols],
                                            a_hi[:, g % SPLIT, cols].bitcast(F32), ALU.subtract).then_inc(lo_ready, 1)
                if g == GROUPS - 2:
                    dve.wait_ge(w_hi_ready, 1)
                    nc.vector.tensor_tensor(w_lo[:], w_raw[:, 0:2 * LAYERS], w_hi[:].bitcast(F32), ALU.subtract)
                    nc.vector.tensor_tensor(wm_parts[:, :, 1, :], w_raw[:, 2 * LAYERS:],
                                            wm_parts[:, :, 0, :].bitcast(F32), ALU.subtract).then_inc(w_lo_ready, 1)
                if g == GROUPS - 3:
                    dve.wait_ge(small_landed, 48)
                    nc.vector.tensor_scalar(two_eps[:], eps_in[:], 1.0, 1.0, ALU.add, ALU.add).then_inc(two_eps_ready, 1)
            dve.wait_ge(two_eps_ready, 1)
            dve.wait_ge(x_res_ready, CHUNKS)
            with dve.Fori(1, LAST) as c:
                split_lo(c, 0)
                split_lo(c, 1)
                ax_lo(c - 1, CW)
                for l in range(LAYERS):
                    split_lo(c, 2 * l + 2)
                    split_lo(c, 2 * l + 3)
                    split_h(c - 1, l, CW)
                for g in range(2 * LAYERS + 2, 2 * LAYERS + 5):
                    split_lo(c, g)
                norm_sum(c - 1, x_raw[:, 0, bass.ds((c - 1) * CT, CT), :], ALL)
                norm_stats(c - 1, ALL)
                dve.wait_ge(stats_done, c)
                split_lo(c, 2 * LAYERS + 5)
                norm_var(ALL)
                split_lo(c, 2 * LAYERS + 6)
                norm_apply(c - 1, ALL)
                for g in range(2 * LAYERS + 7, GROUPS - 1):
                    split_lo(c, g)
                dve.wait_ge(stored, c * 16)
                split_lo(c, GROUPS - 1)

            for half, (s, w) in enumerate(((LAST - 1, CW), (LAST, HW))):
                g = half * (GROUPS // 2)
                split_lo(LAST, g)
                split_lo(LAST, g + 1)
                ax_lo(s, w)
                for l in range(LAYERS):
                    split_lo(LAST, g + 2 * l + 2)
                    split_lo(LAST, g + 2 * l + 3)
                    if half == 1 and l == 0:
                        norm_sum(LAST - 1, x_raw[:, 0, (LAST - 1) * CT:LAST * CT, :], ALL)
                        norm_stats(LAST - 1, ALL)
                        dve.wait_ge(stats_done, LAST)
                        norm_var(ALL)
                    split_h(s, l, w)
                    if half == 1 and l == 0:
                        norm_apply(LAST - 1, ALL)

            norm_sum(LAST, x_raw[:, 0, LAST * CT:LAST * CT + HT, :], HALF)
            norm_stats(LAST, HALF)
            dve.wait_ge(stats_done, LAST + 1)
            norm_var(HALF)
            dve.wait_ge(group_used, CHUNKS * GROUPS)
            nc.vector.tensor_scalar(h[:, 1, HW:], ps_ax_end[1][:, 0:HW], two_eps[:, 1:2], None,
                                    ALU.mult).then_inc(end_h_ready[1], 1)
            dve.wait_ge(stored, LAST * 16)
            norm_apply(LAST, HALF)
            for l in range(LAYERS):
                dve.wait_ge(end_z_done[1], l + 1)
                nc.vector.tensor_scalar(h[:, 1, HW:], ps_z[1][:, HW:], bias[:, 1, l:l + 1], 0.0,
                                        ALU.add, ALU.max).then_inc(end_h_ready[1], 1)
            dve.wait_ge(m_done, LAST + 2)
            nc.vector.tensor_tensor(y[:, OTHER_HALF, :], ps_m_end[:, 0:HW].rearrange("p (t d) -> p t d", d=D),
                                    x_raw[:, 0, LAST * CT + HT:, :], ALU.add).then_inc(y_ready, 1)
            norm_stats(LAST + 1, OTHER_HALF)
            dve.wait_ge(stats_done, LAST + 2)
            norm_var(OTHER_HALF)
            norm_apply(LAST + 1, OTHER_HALF)

        @block.tensor
        def _(pe):
            def matmul3(dst, w_parts, m_parts, start, stop):
                (wh, wl), (mh, ml) = w_parts, m_parts
                nc.tensor.matmul(dst, wh, mh, start=start, stop=False)
                nc.tensor.matmul(dst, wl, mh, start=False, stop=False)
                return nc.tensor.matmul(dst, wh, ml, start=False, stop=stop)

            def adj_branch(ps, b, g, t0, tiles, w):
                for k in range(tiles):
                    t = t0 + k
                    cols = slice(k * w, (k + 1) * w)
                    last = matmul3(ps[b][:, 0:w], (x_hi[:, b, t, :], x_lo[:, b, t, :]),
                                   (a_hi[:, g % SPLIT, cols], a_lo[:, g % SPLIT, cols]), t == 0, t == TILES - 1)
                return last

            def adj_pair(c, l, between=None):
                halves = isinstance(c, int) and c == LAST
                tiles, w = (2 * GK, HW) if halves else (GK, CW)
                in_half = GROUPS // 2 if halves else GROUPS
                ps = ps_ax_end if halves and 2 * l >= in_half else ps_ax
                for b in range(2):
                    if l == 0:
                        pe.wait_ge(h_lo_ready, (c - 1) * (2 * LAYERS + 2) + (b + 1))
                    for g in (2 * l, 2 * l + 1):
                        if b == 0:
                            pe.wait_ge(lo_ready, split_count(c, g))
                        last = adj_branch(ps, b, g, g % in_half * tiles, tiles, w)
                        if b == 1:
                            last.then_inc(group_used, 1)
                        elif g % in_half == in_half - 1:
                            last.then_inc(ax_done, 1)
                    if b == 0 and between:
                        between()

            def layer(s, l, w):
                for b in range(2):
                    pe.wait_ge(h_lo_ready, s * (2 * LAYERS + 2) + (2 * l + b + 1))
                    i = b * LAYERS + l
                    matmul3(ps_z[b][:, 0:w], (w_hi[:, i, :], w_lo[:, i, :]), (h_hi[:, b, 0:w], h_lo[:, b, 0:w]),
                            True, True).then_inc(z_done, 1)

            def merge(s, tiles):
                pe.wait_ge(h_lo_ready, s * (2 * LAYERS + 2) + (2 * LAYERS + 2))
                for t in range(tiles):
                    cols = slice(t * P, (t + 1) * P)
                    dst = ps_m[:, t].rearrange("p a d -> p (a d)")
                    for b in range(2):
                        wm_b = wm_parts[:, b].rearrange("p a d -> p (a d)")
                        nc.tensor.matmul(dst, h_hi[:, b, cols], wm_b, start=b == 0, stop=False)
                        last = nc.tensor.matmul(dst, h_lo[:, b, cols], wm_b, start=False, stop=b == 1)
                last.then_inc(m_done, 1)

            PAIRS = GROUPS // 2

            pe.wait_ge(pe_warm_ready, 1)
            for _ in range(WARM):
                nc.tensor.matmul(ps_z[0][:], pe_warm[:], pe_warm[:, None, :].broadcast_to([P, CT, P]),
                                 start=True, stop=True)

            for t in range(TILES - 2 * GK):
                g, k = divmod(t, GK)
                cols = slice(k * CW, (k + 1) * CW)
                hi, lo = a_hi[:, g % SPLIT, cols], a_lo[:, g % SPLIT, cols]
                if k == 0:
                    pe.wait_ge(x_lo_ready, g + 1)
                pe.wait_ge(hi_ready, t + 1)
                for b in range(2):
                    nc.tensor.matmul(ps_ax[b][:], x_hi[:, b, t, :], hi, start=t == 0, stop=False)
                    nc.tensor.matmul(ps_ax[b][:], x_lo[:, b, t, :], hi, start=False, stop=False)
                pe.wait_ge(lo_ready, t + 1)
                for b in range(2):
                    last = nc.tensor.matmul(ps_ax[b][:], x_hi[:, b, t, :], lo, start=False, stop=False)
                if k == GK - 1:
                    last.then_inc(group_used, 1)
            pe.wait_ge(x_lo_ready, GROUPS)
            pe.wait_ge(lo_ready, TILES)
            for b in range(2):
                for g in (GROUPS - 2, GROUPS - 1):
                    last = adj_branch(ps_ax, b, g, g * GK, GK, CW)
                    if b == 1:
                        last.then_inc(group_used, 1)
                if b == 0:
                    last.then_inc(ax_done, 1)

            pe.wait_ge(w_lo_ready, 1)
            with pe.Fori(1, LAST) as c:
                adj_pair(c, 0)
                for l in range(LAYERS):
                    layer(c - 1, l, CW)
                    adj_pair(c, l + 1)
                merge(c - 1, CT)
                for l in range(LAYERS + 1, PAIRS):
                    adj_pair(c, l)

            for l in range(LAYERS):
                adj_pair(LAST, l)
                layer(LAST - 1, l, CW)
            adj_pair(LAST, LAYERS)
            merge(LAST - 1, CT)
            for l in range(LAYERS):
                adj_pair(LAST, PAIRS // 2 + l)
                layer(LAST, l, HW)
            adj_pair(LAST, PAIRS - 1, between=lambda: merge(LAST, HT))

            for l in range(LAYERS):
                for b in range(2):
                    pe.wait_ge(end_h_ready[b], l + 1)
                    nc.tensor.matmul(ps_z[b][:, HW:], w_raw[:, b * LAYERS + l, :], h[:, b, HW:],
                                     start=True, stop=True).then_inc(end_z_done[b], 1)
            for b in range(2):
                pe.wait_ge(end_h_ready[b], LAYERS + 1)
                for t in range(HT):
                    cols = slice(HW + t * P, HW + (t + 1) * P)
                    last = nc.tensor.matmul(ps_m_end[:, t * D:(t + 1) * D], h[:, b, cols], w_raw[:, 2 * LAYERS + b, :],
                                            start=b == 0 and t == 0, stop=b == 1 and t == HT - 1)
            last.then_inc(m_done, 1)


def kernel(x, adj, L0_gnn_x2, L0_gnn_eps1, L0_gnn_eps2, L0_gnn_W1, L0_gnn_b1, L0_gnn_W2, L0_gnn_b2, L0_gnn_Wm,
           L0_gnn_bm):
    import numpy as np
    import concourse.bacc as bacc
    from concourse.bass_utils import run_bass_kernel_spmd

    n, d = x.shape
    tiles, chunk_tiles, groups = n // P, 4, 16
    chunks, group_tiles, half_tiles = tiles // chunk_tiles, tiles // groups, chunk_tiles // 2
    by_tile = np.asarray(adj).reshape(P, chunks, chunk_tiles, P, tiles).transpose(1, 4, 3, 2, 0)
    blocks = np.empty((chunks, groups, P, group_tiles * chunk_tiles * P), adj.dtype)
    blocks[:-1] = (by_tile[:-1].reshape(chunks - 1, groups, group_tiles, P, chunk_tiles, P)
                   .transpose(0, 1, 3, 2, 4, 5).reshape(blocks[:-1].shape))
    blocks[-1] = (by_tile[-1].reshape(groups // 2, 2 * group_tiles, P, 2, half_tiles, P)
                  .transpose(3, 0, 2, 1, 4, 5).reshape(blocks[-1].shape))
    layers = lambda w: np.asarray(w).transpose(2, 0, 1)
    arrays = {
        "xs": np.stack([np.asarray(x), np.asarray(L0_gnn_x2)]),
        "adj": blocks,
        "eps": np.concatenate([np.asarray(L0_gnn_eps1), np.asarray(L0_gnn_eps2)]),
        "w1": layers(L0_gnn_W1),
        "b1": np.asarray(L0_gnn_b1).T,
        "w2": layers(L0_gnn_W2),
        "b2": np.asarray(L0_gnn_b2).T,
        "wm": np.asarray(L0_gnn_Wm).reshape(d, 2, d).transpose(2, 1, 0),
        "bm": np.asarray(L0_gnn_bm),
    }
    arrays = {f"in_{k}": np.ascontiguousarray(v) for k, v in arrays.items()}
    nc = bacc.Bacc("TRN2", target_bir_lowering=False, num_devices=1)
    args = [nc.dram_tensor(k, v.shape, mybir.dt.from_np(v.dtype), kind="ExternalInput").ap() for k, v in arrays.items()]
    out = nc.dram_tensor("out", (n, d), mybir.dt.float32, kind="ExternalOutput").ap()
    graph_layer_kernel(nc, *args, out)
    r = run_bass_kernel_spmd(nc, [arrays], core_ids=[0])
    return r.results[0]["out"]
```
